# Optimizing a Trainium2 kernel written in Bass

```python
import numpy as np
import jax
import jax.numpy as jnp

def _softmax(x, axis=-1):
    return jax.nn.softmax(x, axis=axis)

def _gelu(x):
    return jax.nn.gelu(x, approximate=True)

def _silu(x):
    return jax.nn.silu(x)

def _sigmoid(x):
    return jax.nn.sigmoid(x)

def _layernorm(x, axis=-1, eps=1e-05):
    m = jnp.mean(x, axis=axis, keepdims=True)
    v = jnp.var(x, axis=axis, keepdims=True)
    return (x - m) / jnp.sqrt(v + eps)

def _scatter_add(tgt, idx, src, axis=0):
    return tgt.at[idx].add(src)

def _segment_sum(src, seg, n):
    return jax.ops.segment_sum(src, seg, n)
kernel_name = 'mk_xattn_ffn_d1_seqx_r8_db309f'

def setup_inputs(seed: int=0):
    np.random.seed(seed)
    _w = jnp.asarray

    def _rec_inputs():
        import jax
        import jax.numpy as jnp
        _rk = jax.random.key(seed)
        x = -0.000125 + 0.9999 * jax.random.normal(jax.random.fold_in(_rk, 1), (4, 512, 128), jnp.float32)
        _lenS = 512 - jax.random.randint(jax.random.fold_in(_rk, 7), (4,), 0, max(1, 512 // 4) + 1, jnp.int32)
        _lenS2 = 77 - jax.random.randint(jax.random.fold_in(_rk, 8), (4,), 0, max(1, 77 // 4) + 1, jnp.int32)
        _ctx_1024P = jax.random.normal(jax.random.fold_in(_rk, 11), (4, 16, 128), jnp.float32)
        _ctx_1024c = jax.random.dirichlet(jax.random.fold_in(_rk, 511), 0.3 * jnp.ones((16,), jnp.float32), (4, 77))
        _ctx_1024t = jnp.einsum('bsk,bkd->bsd', _ctx_1024c, _ctx_1024P)
        _ctx_1024t = _ctx_1024t * jax.lax.rsqrt(jnp.mean(jnp.square(_ctx_1024t)) + 1e-12) * 0.953939
        ctx_1024 = -1.52775e-05 + 0.999936 * (_ctx_1024t + 0.3 * jax.random.normal(jax.random.fold_in(_rk, 611), (4, 77, 128), jnp.float32))
        return (x, ctx_1024)
    x, ctx_1024 = _rec_inputs()

    def _L0_xattn_setup():
        import jax, jax.numpy as jnp
        import numpy as np
        B, S, D = (8, 512, 128)
        key = jax.random.key(seed)
        kq, kk, kv, kw, kb = jax.random.split(key, 5)
        query = jax.random.normal(kq, (B, S, D), dtype=jnp.float32)
        k = jax.random.normal(kk, (B, S, D), dtype=jnp.float32)
        value = jax.random.normal(kv, (B, S, D), dtype=jnp.float32)
        bound = 1.0 / np.sqrt(D)
        W_out = jax.random.uniform(kw, (D, D), minval=-bound, maxval=bound, dtype=jnp.float32)
        b_out = jax.random.uniform(kb, (D,), minval=-bound, maxval=bound, dtype=jnp.float32)
        return {'query': query, 'key': k, 'value': value, 'W_out': W_out, 'b_out': b_out}
    _L0_xattn_all = _L0_xattn_setup()
    _L0_xattn_in = {k: v for k, v in _L0_xattn_all.items() if k in ('W_out', 'b_out')}
    del _L0_xattn_all

    def _L0_ffn_setup():
        import jax, jax.numpy as jnp
        import numpy as np
        H_DIM, E_DIM = (128, 64)
        N_SHARED, N_ROUTED, TOP_K = (2, 16, 4)
        B, S = (4, 256)
        key = jax.random.key(seed)
        ks = jax.random.split(key, 6)
        sc = 1.0 / np.sqrt(H_DIM)
        ec = 1.0 / np.sqrt(E_DIM)
        return {'x': jax.random.normal(ks[0], (B, S, H_DIM), dtype=jnp.float32), 'shared_up': jax.random.uniform(ks[1], (N_SHARED, E_DIM, H_DIM), jnp.float32, -sc, sc), 'shared_down': jax.random.uniform(ks[2], (N_SHARED, H_DIM, E_DIM), jnp.float32, -ec, ec), 'routed_up': jax.random.uniform(ks[3], (N_ROUTED, E_DIM, H_DIM), jnp.float32, -sc, sc), 'routed_down': jax.random.uniform(ks[4], (N_ROUTED, H_DIM, E_DIM), jnp.float32, -ec, ec), 'router_w': jax.random.uniform(ks[5], (N_ROUTED, H_DIM), jnp.float32, -sc, sc)}
    _L0_ffn_all = _L0_ffn_setup()
    _L0_ffn_in = {k: v for k, v in _L0_ffn_all.items() if k in ('shared_up', 'shared_down', 'routed_up', 'routed_down', 'router_w')}
    del _L0_ffn_all
    return {'x': x, 'ctx_1024': ctx_1024, 'L0_xattn_W_out': _L0_xattn_in['W_out'], 'L0_xattn_b_out': _L0_xattn_in['b_out'], 'L0_ffn_shared_up': _L0_ffn_in['shared_up'], 'L0_ffn_shared_down': _L0_ffn_in['shared_down'], 'L0_ffn_routed_up': _L0_ffn_in['routed_up'], 'L0_ffn_routed_down': _L0_ffn_in['routed_down'], 'L0_ffn_router_w': _L0_ffn_in['router_w']}

def reference(x, ctx_1024, L0_xattn_W_out, L0_xattn_b_out, L0_ffn_shared_up, L0_ffn_shared_down, L0_ffn_routed_up, L0_ffn_routed_down, L0_ffn_router_w):
    import jax
    import jax.numpy as jnp

    def _L0_xattn_ref(query, key, value, W_out, b_out):
        import jax, jax.numpy as jnp
        import numpy as np
        B, S, D = (8, 512, 128)
        d = query.shape[-1]
        scale = 1.0 / jnp.sqrt(jnp.asarray(d, dtype=query.dtype))
        scores = jnp.einsum('bqd,bkd->bqk', query, key) * scale
        attn = jax.nn.softmax(scores, axis=-1)
        ctx = jnp.einsum('bqk,bkd->bqd', attn, value)
        out = jnp.einsum('bqd,ed->bqe', ctx, W_out) + b_out
        return out

    def _L0_ffn_ref(x, shared_up, shared_down, routed_up, routed_down, router_w):
        import jax, jax.numpy as jnp
        import numpy as np
        H_DIM, E_DIM = (128, 64)
        N_SHARED, N_ROUTED, TOP_K = (2, 16, 4)
        B, S = (4, 256)
        b, s, h = x.shape
        xt = x.reshape(-1, h)
        up_s = jnp.einsum('th,seh->tse', xt, shared_up)
        shared = jnp.einsum('tse,she->th', jax.nn.gelu(up_s, approximate=False), shared_down)
        probs = jax.nn.softmax(xt @ router_w.T, axis=-1)
        topk_p, topk_i = jax.lax.top_k(probs, TOP_K)
        gate = jnp.zeros_like(probs).at[jnp.arange(xt.shape[0])[:, None], topk_i].add(topk_p)
        up_r = jnp.einsum('th,reh->tre', xt, routed_up)
        act = jax.nn.gelu(up_r, approximate=False) * gate[:, :, None]
        routed = jnp.einsum('tre,rhe->th', act, routed_down)
        return (shared + routed).reshape(b, s, h)
    x = x + _L0_xattn_ref(_layernorm(x, axis=-1), ctx_1024, ctx_1024, L0_xattn_W_out, L0_xattn_b_out)
    x = x + _L0_ffn_ref(_layernorm(x, axis=-1), L0_ffn_shared_up, L0_ffn_shared_down, L0_ffn_routed_up, L0_ffn_routed_down, L0_ffn_router_w)
    return x

_drawn_inputs = setup_inputs


def setup_inputs(seed=0):
    import zlib

    import numpy as np

    out = dict(_drawn_inputs(seed))
    spreads = {}
    factors = {}
    for name, (base, spread) in spreads.items():
        noise = np.random.default_rng([zlib.crc32(name.encode()), seed]).standard_normal(out[name].shape)
        drawn = base * np.exp(spread * noise) if base else spread * noise
        out[name] = jnp.asarray(drawn.astype(out[name].dtype))
    for name, factor in factors.items():
        out[name] = (out[name] * factor).astype(out[name].dtype)
    return out
```

```python
import concourse.bass as bass
from concourse import mybir
from contextlib import ExitStack

B, S, D = 4, 512, 128
KEYS = 77
E_DIM, N_SHARED, N_ROUTED = 64, 2, 16
TOP_K = 4
EPS = 1e-5
P = 128
J = S // P
HID = (N_SHARED + N_ROUTED) * E_DIM
C = HID // P
N_CHUNKS = B * C

SPLIT = (False, True, True, False, True, True, False, True, True)
LAG = 3
N_ACT, N_GATED, N_PARTS = 4, 4, 4

SPLITS = [g for g in range(N_CHUNKS) if SPLIT[g % C]]
GATED = [g for g in range(N_CHUNKS) if g % C]


def xattn_moe_kernel(nc, xT, x, attn_pack, b_out, upT, downT, selector, identity, out):
    f32, f32r = mybir.dt.float32, mybir.dt.float32r
    ALU, ACT, AX = mybir.AluOpType, mybir.ActivationFunctionType, mybir.AxisListType

    ctx = ExitStack()
    with ctx:
        def sb(name, shape, dt=f32):
            return ctx.enter_context(nc.sbuf_tensor(name, shape, dt))

        def bank(name):
            return ctx.enter_context(nc.psum_tensor(name, [P, 512], f32))

        def sem(name):
            return ctx.enter_context(nc.semaphore(name))

        xT_sb = sb("xT_sb", [P, B, S])
        x_sb = sb("x_sb", [P, B, J, D])
        pack_sb = sb("pack_sb", [P, B * KEYS + D + N_ROUTED])
        ctxT = pack_sb[:, 0:B * KEYS]
        woT = pack_sb[:, B * KEYS:B * KEYS + D]
        rwT = pack_sb[:, B * KEYS + D:]
        bout_sb = sb("bout_sb", [1, D])
        ones_row = sb("ones_row", [1, KEYS])
        mean_mat = sb("mean_mat", [P, P])
        ident = sb("ident", [P, P])
        sel_f = sb("sel_f", [2 * N_ROUTED, C - 1, P])
        sel = sb("sel", [2 * N_ROUTED, C - 1, P], f32r)
        up_f = sb("up_f", [P, C, P])
        up_hi = sb("up_hi", [P, C, P], f32r)
        up_lo = sb("up_lo", [P, C, P], f32r)
        down_f = sb("down_f", [P, C, D])
        down_hi = sb("down_hi", [P, C, D], f32r)
        down_lo = sb("down_lo", [P, C, D], f32r)
        kc = sb("kc", [P, B * KEYS])
        vproj = sb("vproj", [KEYS, B, D])
        mhalf = sb("mhalf", [P, J])
        bn1 = sb("bn1", [P, B, J, 6])
        mv1 = sb("mv1", [P, B, J, 2])
        var1 = sb("var1", [P, B, J])
        rs1 = sb("rs1", [P, B, J])
        nmax = sb("nmax", [P, B, J])
        nbias = sb("nbias", [P, B, J])
        prob = sb("prob", [P, B, J, KEYS])
        den = sb("den", [P, B, J])
        rden = sb("rden", [P, B, J])
        probT = sb("probT", [KEYS, B, S])
        x1 = sb("x1", [P, B, J, D])
        bn2 = sb("bn2", [P, B, J, 6])
        mv2 = sb("mv2", [P, B, J, 2])
        var2 = sb("var2", [P, B, J])
        rs2 = sb("rs2", [P, B, J])
        xn2 = sb("xn2", [P, B, J, D])
        xn_hi = sb("xn_hi", [P, B, S], f32r)
        xn_lo = sb("xn_lo", [P, B, S], f32r)
        xn_f = sb("xn_f", [P, B, S])
        NSENT = 4
        lmax = sb("lmax", [P, B, J])
        dlog = sb("dlog", [P, B, J, N_ROUTED + NSENT])
        top = sb("top", [P, B, J, 12])
        left = sb("left", [P, B, J, N_ROUTED + NSENT])
        expl = sb("expl", [P, B, J, N_ROUTED])
        esum = sb("esum", [P, B, J])
        resum = sb("resum", [P, B, J])
        chosen = sb("chosen", [P, B, J, N_ROUTED])
        gnum = sb("gnum", [P, B, J, N_ROUTED])
        gate = sb("gate", [P, B, J, N_ROUTED])
        gate2 = sb("gate2", [P, B, J, 2, N_ROUTED], f32r)
        gateT = sb("gateT", [2 * N_ROUTED, B, S], f32r)
        act_r = sb("act_r", [P, N_ACT, S])
        gated_r = sb("gated_r", [P, N_GATED, S])
        hi_r = sb("hi_r", [P, N_PARTS, S], f32r)
        lo_r = sb("lo_r", [P, N_PARTS, S], f32r)
        ffnT = sb("ffnT", [P, B, S])
        out_sb = sb("out_sb", [P, B, J, D])

        up_ps = [bank("up0"), bank("up1")]
        gb_ps = [bank("gb0"), bank("gb1")]
        down_ps, bank_a, bank_b, bank_c = bank("down"), bank("bank_a"), bank("bank_b"), bank("bank_c")
        score_ps = [bank_a, bank_b, gb_ps[0], gb_ps[1]]

        def tiles(ps, w):
            return ps[:, 0:J * w].rearrange("p (j w) -> p j w", w=w)

        ld_xT0, ld_pack, ld_x0, ld_xT, ld_x = map(sem, ("ld_xT0", "ld_pack", "ld_x0", "ld_xT", "ld_x"))
        ld_bout, ld_up, ld_down, ld_sel, ld_id = map(sem, ("ld_bout", "ld_up", "ld_down", "ld_sel", "ld_id"))
        const_ready, kbar_done, kc_ready, vproj_done, vproj_ready = map(sem, (
            "const_ready", "kbar_done", "kc_ready", "vproj_done", "vproj_ready"))
        uphi_ready, uplo_ready, dnhi_ready, dnlo_ready, sel_ready = map(sem, (
            "uphi_ready", "uplo_ready", "dnhi_ready", "dnlo_ready", "sel_ready"))
        scores_done, bn1_tiles, mv1_tiles, var1_ready, rs1_ready = map(sem, (
            "scores_done", "bn1_tiles", "mv1_tiles", "var1_ready", "rs1_ready"))
        nmax_ready, nbias_ready, prob_tiles, probT_done, probT_ready = map(sem, (
            "nmax_ready", "nbias_ready", "prob_tiles", "probT_done", "probT_ready"))
        attn_done, rden_ready, x1_tiles, bn2_tiles, mv2_tiles, var2_ready, rs2_ready, xn2_tiles = map(sem, (
            "attn_done", "rden_ready", "x1_tiles", "bn2_tiles", "mv2_tiles", "var2_ready", "rs2_ready", "xn2_tiles"))
        xnT_done, xnhi_ready, xnf_ready, xnlo_ready = map(sem, (
            "xnT_done", "xnhi_ready", "xnf_ready", "xnlo_ready"))
        logits_done, lmax_ready, dlog_ready, top_tiles, left_tiles, expl_ready = map(sem, (
            "logits_done", "lmax_ready", "dlog_ready", "top_tiles", "left_tiles", "expl_ready"))
        esum_ready, resum_ready, chosen_ready, gnum_ready, gate_ready, ghi_ready, glo_ready = map(sem, (
            "esum_ready", "resum_ready", "chosen_ready", "gnum_ready", "gate_ready", "ghi_ready", "glo_ready"))
        gateT_done, gateT_ready = map(sem, ("gateT_done", "gateT_ready"))
        up_chunks, act_chunks, gb_chunks, gated_chunks, hi_chunks, lo_chunks, down_chunks = map(sem, (
            "up_chunks", "act_chunks", "gb_chunks", "gated_chunks", "hi_chunks", "lo_chunks", "down_chunks"))
        ffnT_ready, outT_done, out_ready, stored = map(sem, ("ffnT_ready", "outT_done", "out_ready", "stored"))

        AT_PROBT, AT_ATTN, AT_XNT, AT_LOGITS, AT_GATET = 0, 1, 3, 4, 6
        AT_OUT = LAG

        def stage_batch(g, at):
            b = g // C + 1
            return b if g % C == at and b < B else None

        def source(g):
            if g % C == 0:
                return act_r[:, g % N_ACT, :]
            return gated_r[:, GATED.index(g) % N_GATED, :]

        def wait_source(eng, g):
            if g % C == 0:
                eng.wait_ge(act_chunks, g + 1)
            else:
                eng.wait_ge(gated_chunks, GATED.index(g) + 1)

        def wait_source_free(eng, g):
            if SPLIT[g % C]:
                eng.wait_ge(lo_chunks, SPLITS.index(g) + 1)
            else:
                eng.wait_ge(down_chunks, g + 1)

        block = ctx.enter_context(nc.Block())

        @block.sync
        def _(sp):
            sp.dma_start(xT_sb[:, 0, :], xT[:, 0, :]).then_inc(ld_xT0, 16)
            sp.dma_start(pack_sb[:, :], attn_pack).then_inc(ld_pack, 16)
            sp.dma_start(ident[:, :], identity).then_inc(ld_id, 16)
            sp.dma_start(xT_sb[:, 1:B, :], xT[:, 1:B, :]).then_inc(ld_xT, 16)
            sp.dma_start(up_f[:, :, :], upT).then_inc(ld_up, 16)
            sp.dma_start(down_f[:, :, :], downT).then_inc(ld_down, 16)
            for b in range(B):
                sp.wait_ge(out_ready, b + 1)
                sp.dma_start(out[b], out_sb[:, b, :, :]).then_inc(stored, 16)
            sp.wait_ge(stored, 16 * B)

        @block.gpsimd
        def _(pool):
            pool.memset(mean_mat[:, :], 1.0 / D).then_inc(const_ready, 1)
            pool.memset(ones_row[:, :], 1.0).then_inc(const_ready, 1)
            pool.memset(mhalf[:, :], -0.5).then_inc(const_ready, 1)
            pool.memset(dlog[:, :, :, N_ROUTED:], -3.0e38).then_inc(const_ready, 1)
            pool.memset(top[:, :, :, 8:], -3.0e38).then_inc(const_ready, 1)
            pool.wait_ge(const_ready, 5)

            def rstd(b, mv, var, rs, mv_tiles, var_sem, rs_sem, factor):
                pool.wait_ge(mv_tiles, J * (b + 1))
                nc.gpsimd.tensor_scalar(var[:, b, :], mv[:, b, :, 1], EPS, factor,
                                        ALU.add, ALU.mult).then_inc(var_sem, 1)
                pool.wait_ge(var_sem, b + 1)
                nc.gpsimd.tensor_tensor(rs[:, b, :], var[:, b, :], mhalf[:, :], ALU.pow).then_inc(rs_sem, 1)

            def rstd1(b):
                rstd(b, mv1, var1, rs1, mv1_tiles, var1_ready, rs1_ready, float(D))

            def rstd2(b):
                rstd(b, mv2, var2, rs2, mv2_tiles, var2_ready, rs2_ready, 1.0)

            rstd1(0)
            pool.wait_ge(ld_sel, 16)
            nc.gpsimd.tensor_copy(sel[:, :, :], sel_f[:, :, :]).then_inc(sel_ready, 1)
            rstd1(1)
            rstd2(0)
            rstd1(2)
            pool.wait_ge(uphi_ready, 1)
            nc.gpsimd.tensor_tensor(up_lo[:, :, :], up_f[:, :, :], up_hi[:, :, :].bitcast(f32),
                                    ALU.subtract).then_inc(uplo_ready, 1)
            rstd1(3)
            pool.wait_ge(dnhi_ready, 1)
            nc.gpsimd.tensor_tensor(down_lo[:, :, :], down_f[:, :, :], down_hi[:, :, :].bitcast(f32),
                                    ALU.subtract).then_inc(dnlo_ready, 1)
            for g in range(N_CHUNKS):
                if (b := stage_batch(g, AT_ATTN)) is not None:
                    rstd2(b)
                if SPLIT[g % C]:
                    s = SPLITS.index(g)
                    pool.wait_ge(hi_chunks, s + 1)
                    if s >= N_PARTS:
                        pool.wait_ge(down_chunks, SPLITS[s - N_PARTS] + 1)
                    nc.gpsimd.tensor_tensor(lo_r[:, s % N_PARTS, :], source(g),
                                            hi_r[:, s % N_PARTS, :].bitcast(f32),
                                            ALU.subtract).then_inc(lo_chunks, 1)

        @block.scalar
        def _(act):
            act.dma_start(x_sb[:, 0, :, :], x[0]).then_inc(ld_x0, 16)
            act.dma_start(bout_sb[:, :], b_out).then_inc(ld_bout, 16)
            act.dma_start(x_sb[:, 1:B, :, :], x[1:B].rearrange("b p j d -> p b j d")).then_inc(ld_x, 16)
            act.dma_start(sel_f[:, :, :], selector).then_inc(ld_sel, 16)
            nc.scalar.preload_act_table(ACT.Exp)

            def softmax_exp(b):
                act.wait_ge(scores_done, b + 1)
                act.wait_ge(nbias_ready, b + 1)
                for j in range(J):
                    nc.scalar.activation(prob[:, b, j, :], tiles(score_ps[b], KEYS)[:, j, :], ACT.Exp,
                                         bias=nbias[:, b, j:j + 1], scale=rs1[:, b, j:j + 1],
                                         accum_out=den[:, b, j:j + 1]).then_inc(prob_tiles, 1)

            def copy_probT(b):
                act.wait_ge(probT_done, b + 1)
                nc.scalar.copy(probT[:, b, :], bank_b[0:KEYS, :]).then_inc(probT_ready, 1)

            def copy_xnT(b):
                act.wait_ge(xnT_done, b + 1)
                nc.scalar.copy(xn_hi[:, b, :], bank_b[:, :]).then_inc(xnhi_ready, 1)
                nc.scalar.copy(xn_f[:, b, :], bank_b[:, :]).then_inc(xnf_ready, 1)

            def router_exp(b):
                act.wait_ge(dlog_ready, b + 1)
                nc.scalar.activation(expl[:, b, :, :], dlog[:, b, :, 0:N_ROUTED], ACT.Exp).then_inc(expl_ready, 1)

            def copy_gateT(b):
                act.wait_ge(gateT_done, b + 1)
                nc.scalar.copy(gateT[:, b, :], bank_a[0:2 * N_ROUTED, :]).then_inc(gateT_ready, 1)

            def copy_ffnT(b):
                act.wait_ge(down_chunks, C * (b + 1))
                nc.scalar.copy(ffnT[:, b, :], down_ps[:, :]).then_inc(ffnT_ready, 1)

            softmax_exp(0)
            act.wait_ge(vproj_done, 1)
            nc.scalar.copy(vproj[:, :, :], tiles(up_ps[1], D)[0:KEYS, :, :]).then_inc(vproj_ready, 1)
            softmax_exp(1)
            copy_probT(0)
            act.wait_ge(ld_up, 16)
            nc.scalar.copy(up_hi[:, :, :], up_f[:, :, :]).then_inc(uphi_ready, 1)
            softmax_exp(2)
            copy_xnT(0)
            softmax_exp(3)
            router_exp(0)
            for g in range(N_CHUNKS + LAG + 1):
                if g < N_CHUNKS:
                    if (b := stage_batch(g, AT_PROBT)) is not None:
                        copy_probT(b)
                    if (b := stage_batch(g, AT_XNT)) is not None:
                        copy_xnT(b)
                    if (b := stage_batch(g, AT_LOGITS + 1)) is not None:
                        router_exp(b)
                    if (b := stage_batch(g, AT_GATET)) is not None:
                        copy_gateT(b)
                    act.wait_ge(up_chunks, g + 1)
                    if g >= N_ACT:
                        if (g - N_ACT) % C:
                            act.wait_ge(gated_chunks, GATED.index(g - N_ACT) + 1)
                        else:
                            wait_source_free(act, g - N_ACT)
                    nc.scalar.activation(act_r[:, g % N_ACT, :], up_ps[g % 2][:, :], ACT.Gelu).then_inc(act_chunks, 1)
                    if g == 0:
                        copy_gateT(0)
                        act.wait_ge(ld_down, 16)
                        nc.scalar.copy(down_hi[:, :, :], down_f[:, :, :]).then_inc(dnhi_ready, 1)
                if g >= 1 and g - 1 in SPLITS:
                    s = SPLITS.index(g - 1)
                    wait_source(act, g - 1)
                    if s >= N_PARTS:
                        act.wait_ge(down_chunks, SPLITS[s - N_PARTS] + 1)
                    nc.scalar.copy(hi_r[:, s % N_PARTS, :], source(g - 1)).then_inc(hi_chunks, 1)
                if g >= C + LAG - 1 and (g - LAG + 1) % C == 0:
                    copy_ffnT((g - LAG + 1) // C - 1)

        @block.vector
        def _(dve):
            def stats(b, src, bn, mv, bn_sem, mv_sem):
                for j in range(J):
                    nc.vector.bn_stats(bn[:, b, j, :], src[:, b, j, :]).then_inc(bn_sem, 1)
                for j in range(J):
                    dve.wait_ge(bn_sem, J * b + j + 1)
                    nc.vector.bn_aggr(mv[:, b, j, :], bn[:, b, j, :]).then_inc(mv_sem, 1)

            def attention_head(b):
                dve.wait_ge(ld_x if b else ld_x0, 16)
                stats(b, x_sb, bn1, mv1, bn1_tiles, mv1_tiles)
                if b == 0:
                    dve.wait_ge(ld_pack, 16)
                    dve.wait_ge(kbar_done, 1)
                    nc.vector.tensor_tensor(kc[:, :], ctxT, up_ps[0][:, 0:B * KEYS], ALU.subtract).then_inc(kc_ready, 1)
                dve.wait_ge(scores_done, b + 1)
                nc.vector.tensor_reduce(nmax[:, b, :], tiles(score_ps[b], KEYS), AX.X, ALU.max,
                                        negate=True).then_inc(nmax_ready, 1)
                dve.wait_ge(nmax_ready, b + 1)
                dve.wait_ge(rs1_ready, b + 1)
                nc.vector.tensor_tensor(nbias[:, b, :], nmax[:, b, :], rs1[:, b, :],
                                        ALU.mult).then_inc(nbias_ready, 1)

            def attention_out(b):
                dve.wait_ge(prob_tiles, J * (b + 1))
                nc.vector.reciprocal(rden[:, b, :], den[:, b, :]).then_inc(rden_ready, 1)
                dve.wait_ge(attn_done, b + 1)
                dve.wait_ge(rden_ready, b + 1)
                for j in range(J):
                    nc.vector.scalar_tensor_tensor(x1[:, b, j, :], tiles(bank_c, D)[:, j, :], rden[:, b, j:j + 1],
                                                   x_sb[:, b, j, :], ALU.mult, ALU.add).then_inc(x1_tiles, 1)
                dve.wait_ge(x1_tiles, J * (b + 1))
                stats(b, x1, bn2, mv2, bn2_tiles, mv2_tiles)
                dve.wait_ge(mv2_tiles, J * (b + 1))
                dve.wait_ge(rs2_ready, b + 1)
                for j in range(J):
                    nc.vector.tensor_scalar(xn2[:, b, j, :], x1[:, b, j, :], mv2[:, b, j, 0:1], rs2[:, b, j:j + 1],
                                            ALU.subtract, ALU.mult).then_inc(xn2_tiles, 1)

            def split_xnT(b):
                dve.wait_ge(xnhi_ready, b + 1)
                dve.wait_ge(xnf_ready, b + 1)
                nc.vector.tensor_tensor(xn_lo[:, b, :], bank_b[:, :], xn_hi[:, b, :].bitcast(f32),
                                        ALU.subtract).then_inc(xnlo_ready, 1)

            def spread(v):
                return v.unsqueeze(2).to_broadcast([P, J, N_ROUTED])

            def router_choose(b):
                dve.wait_ge(logits_done, b + 1)
                logits = tiles(bank_a, N_ROUTED)
                nc.vector.tensor_reduce(lmax[:, b, :], logits, AX.X, ALU.max).then_inc(lmax_ready, 1)
                dve.wait_ge(lmax_ready, b + 1)
                if b == 0:
                    dve.wait_ge(const_ready, 5)
                nc.vector.tensor_tensor(dlog[:, b, :, 0:N_ROUTED], logits, spread(lmax[:, b, :]),
                                        ALU.subtract).then_inc(dlog_ready, 1)
                dve.wait_ge(dlog_ready, b + 1)
                for j in range(J):
                    nc.vector.max(top[:, b, j, 0:8], dlog[:, b, j, 0:N_ROUTED]).then_inc(top_tiles, 1)
                for j in range(J):
                    dve.wait_ge(top_tiles, J * b + j + 1)
                    four = top[:, b, j, :].rearrange("p (a k) -> p a k", k=TOP_K)[:, 0:3:2, :]
                    nc.vector.match_replace(left[:, b, j, :], four, dlog[:, b, j, :], 1.0).then_inc(left_tiles, 1)

            def router_gate(b):
                dve.wait_ge(left_tiles, J * (b + 1))
                nc.vector.tensor_tensor(chosen[:, b, :, :], left[:, b, :, 0:N_ROUTED], dlog[:, b, :, 0:N_ROUTED],
                                        ALU.not_equal).then_inc(chosen_ready, 1)
                dve.wait_ge(expl_ready, b + 1)
                nc.vector.tensor_reduce(esum[:, b, :], expl[:, b, :, :], AX.X, ALU.add).then_inc(esum_ready, 1)
                dve.wait_ge(chosen_ready, b + 1)
                nc.vector.tensor_tensor(gnum[:, b, :, :], chosen[:, b, :, :], expl[:, b, :, :],
                                        ALU.mult).then_inc(gnum_ready, 1)
                dve.wait_ge(esum_ready, b + 1)
                nc.vector.reciprocal(resum[:, b, :], esum[:, b, :]).then_inc(resum_ready, 1)
                dve.wait_ge(gnum_ready, b + 1)
                dve.wait_ge(resum_ready, b + 1)
                nc.vector.tensor_tensor(gate[:, b, :, :], gnum[:, b, :, :], spread(resum[:, b, :]),
                                        ALU.mult).then_inc(gate_ready, 1)
                dve.wait_ge(gate_ready, b + 1)
                nc.vector.tensor_copy(gate2[:, b, :, 0, :], gate[:, b, :, :]).then_inc(ghi_ready, 1)
                dve.wait_ge(ghi_ready, b + 1)
                nc.vector.tensor_tensor(gate2[:, b, :, 1, :], gate[:, b, :, :], gate2[:, b, :, 0, :].bitcast(f32),
                                        ALU.subtract).then_inc(glo_ready, 1)

            def finish(b):
                dve.wait_ge(outT_done, b + 1)
                nc.vector.tensor_tensor(out_sb[:, b, :, :], tiles(bank_c, D), x1[:, b, :, :],
                                        ALU.add).then_inc(out_ready, 1)

            attention_head(0)
            attention_head(1)
            attention_out(0)
            attention_head(2)
            split_xnT(0)
            router_choose(0)
            attention_head(3)
            router_gate(0)
            for g in range(N_CHUNKS + LAG + 1):
                if g < N_CHUNKS:
                    if (b := stage_batch(g, AT_ATTN)) is not None:
                        attention_out(b)
                    if (b := stage_batch(g, AT_XNT)) is not None:
                        split_xnT(b)
                    if (b := stage_batch(g, AT_LOGITS)) is not None:
                        router_choose(b)
                    if (b := stage_batch(g, AT_LOGITS + 1)) is not None:
                        router_gate(b)
                    if g % C:
                        r = GATED.index(g)
                        dve.wait_ge(act_chunks, g + 1)
                        dve.wait_ge(gb_chunks, r + 1)
                        if r >= N_GATED:
                            wait_source_free(dve, GATED[r - N_GATED])
                        nc.vector.tensor_tensor(gated_r[:, r % N_GATED, :], act_r[:, g % N_ACT, :],
                                                gb_ps[r % 2][:, :], ALU.mult).then_inc(gated_chunks, 1)
                if g >= C + LAG and (g - LAG) % C == 0:
                    finish((g - LAG) // C - 1)

        @block.tensor
        def _(pe):
            def scores(b):
                if b == 1:
                    pe.wait_ge(ld_xT, 16)
                for j in range(J):
                    last = nc.tensor.matmul(tiles(score_ps[b], KEYS)[:, j, :], xT_sb[:, b, j * P:(j + 1) * P],
                                            kc[:, b * KEYS:(b + 1) * KEYS], start=True, stop=True)
                last.then_inc(scores_done, 1)

            def transpose_prob(b):
                pe.wait_ge(prob_tiles, J * (b + 1))
                if b == 0:
                    pe.wait_ge(ld_id, 16)
                    pe.wait_ge(prob_tiles, 2 * J)
                else:
                    pe.wait_ge(xnlo_ready, b)
                for j in range(J):
                    last = nc.tensor.transpose(bank_b[0:KEYS, j * P:(j + 1) * P], prob[:, b, j, :], ident[:, :])
                last.then_inc(probT_done, 1)

            def attend(b):
                pe.wait_ge(probT_ready, b + 1)
                if b == 0:
                    pe.wait_ge(vproj_ready, 1)
                if b >= 3:
                    pe.wait_ge(out_ready, b - 2)
                for j in range(J):
                    last = nc.tensor.matmul(tiles(bank_c, D)[:, j, :], probT[:, b, j * P:(j + 1) * P],
                                            vproj[:, b, :], start=True, stop=True)
                last.then_inc(attn_done, 1)

            def transpose_xn(b):
                for j in range(J):
                    pe.wait_ge(xn2_tiles, J * b + j + 1)
                    last = nc.tensor.transpose(bank_b[:, j * P:(j + 1) * P], xn2[:, b, j, :], ident[:, :])
                last.then_inc(xnT_done, 1)

            def logits(b):
                pe.wait_ge(xnf_ready, b + 1)
                if b >= 1:
                    pe.wait_ge(gateT_ready, b)
                for j in range(J):
                    last = nc.tensor.matmul(tiles(bank_a, N_ROUTED)[:, j, :], xn_f[:, b, j * P:(j + 1) * P],
                                            rwT, start=True, stop=True)
                last.then_inc(logits_done, 1)

            def transpose_gate(b):
                pe.wait_ge(glo_ready, b + 1)
                for j in range(J):
                    last = nc.tensor.transpose(
                        bank_a[0:2 * N_ROUTED, j * P:(j + 1) * P],
                        gate2[:, b, j, :, :].bitcast(f32).rearrange("p a e -> p (a e)"), ident[:, :])
                last.then_inc(gateT_done, 1)

            def up(g):
                b, c = g // C, g % C
                if c == 0:
                    pe.wait_ge(xnlo_ready, b + 1)
                if g >= 2:
                    pe.wait_ge(act_chunks, g - 1)
                nc.tensor.matmul(up_ps[g % 2][:, :], up_hi[:, c, :], xn_hi[:, b, :], start=True, stop=False)
                nc.tensor.matmul(up_ps[g % 2][:, :], up_hi[:, c, :], xn_lo[:, b, :], start=False, stop=False)
                nc.tensor.matmul(up_ps[g % 2][:, :], up_lo[:, c, :], xn_hi[:, b, :], start=False,
                                 stop=True).then_inc(up_chunks, 1)

            def spread_gate(g):
                b, c = g // C, g % C
                if c == 0:
                    return
                r = GATED.index(g)
                if c == 1:
                    pe.wait_ge(gateT_ready, b + 1)
                if r >= 2:
                    pe.wait_ge(gated_chunks, r - 1)
                nc.tensor.matmul(gb_ps[r % 2][:, :], sel[:, c - 1, :], gateT[:, b, :], start=True,
                                 stop=True).then_inc(gb_chunks, 1)

            def down(g):
                b, c = g // C, g % C
                if c == 0 and b:
                    pe.wait_ge(ffnT_ready, b)
                first, last = c == 0, c == C - 1
                if SPLIT[c]:
                    s = SPLITS.index(g)
                    pe.wait_ge(lo_chunks, s + 1)
                    hi, lo = hi_r[:, s % N_PARTS, :], lo_r[:, s % N_PARTS, :]
                    nc.tensor.matmul(down_ps[:, :], down_hi[:, c, :], hi, start=first, stop=False)
                    nc.tensor.matmul(down_ps[:, :], down_lo[:, c, :], hi, start=False, stop=False)
                    mm = nc.tensor.matmul(down_ps[:, :], down_hi[:, c, :], lo, start=False, stop=last)
                else:
                    wait_source(pe, g)
                    mm = nc.tensor.matmul(down_ps[:, :], down_f[:, c, :], source(g), start=first, stop=last)
                mm.then_inc(down_chunks, 1)

            def transpose_out(b):
                pe.wait_ge(ffnT_ready, b + 1)
                pe.wait_ge(x1_tiles, J * min(b + 3, B))
                for j in range(J):
                    last = nc.tensor.transpose(tiles(bank_c, D)[:, j, :], ffnT[:, b, j * P:(j + 1) * P], ident[:, :])
                last.then_inc(outT_done, 1)

            pe.wait_ge(const_ready, 5)
            pe.wait_ge(ld_pack, 16)
            nc.tensor.matmul(up_ps[0][:, 0:B * KEYS], mean_mat[:, :], ctxT, start=True, stop=True).then_inc(kbar_done, 1)
            pe.wait_ge(ld_bout, 16)
            for b in range(B):
                row = tiles(up_ps[1], D)[0:KEYS, b, :]
                nc.tensor.matmul(row, pack_sb[:, b * KEYS:(b + 1) * KEYS], woT, start=True, stop=False)
                last = nc.tensor.matmul(row, ones_row[:, :], bout_sb[:, :], start=False, stop=True)
            last.then_inc(vproj_done, 1)
            pe.wait_ge(kc_ready, 1)
            pe.wait_ge(ld_xT0, 16)
            scores(0)
            scores(1)
            scores(2)
            scores(3)
            transpose_prob(0)
            attend(0)
            transpose_xn(0)
            logits(0)
            pe.wait_ge(uplo_ready, 1)
            for g in range(N_CHUNKS + LAG + 1):
                if g < N_CHUNKS:
                    if g == 1:
                        pe.wait_ge(sel_ready, 1)
                        transpose_gate(0)
                    if (b := stage_batch(g, AT_PROBT)) is not None:
                        transpose_prob(b)
                    if (b := stage_batch(g, AT_ATTN)) is not None:
                        attend(b)
                    if (b := stage_batch(g, AT_XNT)) is not None:
                        transpose_xn(b)
                    if (b := stage_batch(g, AT_LOGITS)) is not None:
                        logits(b)
                    if (b := stage_batch(g, AT_GATET)) is not None:
                        transpose_gate(b)
                    up(g)
                    spread_gate(g)
                if LAG <= g < N_CHUNKS + LAG:
                    if g == LAG:
                        pe.wait_ge(dnlo_ready, 1)
                    down(g - LAG)
                if g >= C + LAG and (g - LAG) % C == 0:
                    transpose_out((g - LAG) // C - 1)


def kernel(x, ctx_1024, L0_xattn_W_out, L0_xattn_b_out, L0_ffn_shared_up, L0_ffn_shared_down,
           L0_ffn_routed_up, L0_ffn_routed_down, L0_ffn_router_w):
    import numpy as np
    import concourse.bacc as bacc
    from concourse.bass_utils import run_bass_kernel_spmd

    x = np.asarray(x)
    tiles = x.reshape(B, P, J, D)
    up = np.concatenate([np.asarray(L0_ffn_shared_up), np.asarray(L0_ffn_routed_up)])
    down = np.concatenate([np.asarray(L0_ffn_shared_down), np.asarray(L0_ffn_routed_down)])
    selector = np.zeros((2, N_ROUTED, C - 1, P), np.float32)
    for c in range(C - 1):
        for m in range(P):
            selector[:, (c * P + m) // E_DIM, c, m] = 1.0
    arrays = {
        "xT": tiles.transpose(3, 0, 2, 1).reshape(D, B, S),
        "x": tiles,
        "attn_pack": np.concatenate([np.asarray(ctx_1024).transpose(2, 0, 1).reshape(D, B * KEYS),
                                     np.asarray(L0_xattn_W_out).T, np.asarray(L0_ffn_router_w).T], axis=1),
        "b_out": np.asarray(L0_xattn_b_out).reshape(1, D),
        "upT": up.reshape(C, P, D).transpose(2, 0, 1),
        "downT": down.transpose(0, 2, 1).reshape(C, P, D).transpose(1, 0, 2),
        "selector": selector.reshape(2 * N_ROUTED, C - 1, P),
        "identity": np.eye(P, dtype=np.float32),
    }
    arrays = {k + "_dram": np.ascontiguousarray(v) for k, v in arrays.items()}
    nc = bacc.Bacc("TRN2", target_bir_lowering=False, num_devices=1)
    args = [nc.dram_tensor(k, v.shape, mybir.dt.float32, kind="ExternalInput").ap() for k, v in arrays.items()]
    out = nc.dram_tensor("out_dram", (B, P, J, D), mybir.dt.float32, kind="ExternalOutput").ap()
    xattn_moe_kernel(nc, *args, out)
    r = run_bass_kernel_spmd(nc, [arrays], core_ids=[0])
    return r.results[0]["out_dram"].reshape(B, S, D)
```

```python
import concourse.bass as bass
from concourse import mybir
from contextlib import ExitStack

B, S, D = 4, 512, 128
KEYS = 77
E_DIM, N_SHARED, N_ROUTED = 64, 2, 16
TOP_K = 4
EPS = 1e-5
P = 128
J = S // P
HID = (N_SHARED + N_ROUTED) * E_DIM
C = HID // P
N_CHUNKS = B * C

N_ACT, N_GATED, N_PARTS = 7, 6, 9

LAG = 5
SPREAD_LAG = 1
OUT_AFTER = 3
HI_ON_VECTOR = (1, 3, 4, 6, 8)
WHOLE = 2
UP_FIRST = 5
GATE0, GATE0_COPY = 1, 1

PROBT = (-1, 7, 17)
ATTN = (-1, 9, 19)
X1 = (-1, 8, 18)
STATS = (-1, 9, 18)
RSTD = (1, 9, 18)
NORM = (2, 11, 21)
XNT = (6, 14, 24)
SPLIT = (6, 14, 23)
LOGITS = (7, 16, 25)
CHOOSE = (6, 15, 24)
EXPL = (8, 16, 26)
GATE = (7, 15, 25)
GATET = (10, 18, 28)

GATED = [g for g in range(N_CHUNKS) if g % C]


def stage_batch(g, slots):
    return slots.index(g) + 1 if g in slots else None


def is_split(g):
    return g < N_CHUNKS - WHOLE


def on_vector(g):
    return g % C in HI_ON_VECTOR


def finished_batch(g, after):
    b = (g - LAG - after + 1) // C - 1
    return b if (g - LAG - after + 1) % C == 0 and 0 <= b < B else None


def xattn_moe_kernel(nc, xT, x, ctxT_in, attn_pack, b_out, upT, downT, selector, identity, out):
    f32, f32r = mybir.dt.float32, mybir.dt.float32r
    ALU, ACT, AX = mybir.AluOpType, mybir.ActivationFunctionType, mybir.AxisListType

    ctx = ExitStack()
    with ctx:
        def sb(name, shape, dt=f32):
            return ctx.enter_context(nc.sbuf_tensor(name, shape, dt))

        def bank(name):
            return ctx.enter_context(nc.psum_tensor(name, [P, 512], f32))

        def sem(name):
            return ctx.enter_context(nc.semaphore(name))

        xT_sb = sb("xT_sb", [P, B, S])
        x_sb = sb("x_sb", [P, B, J, D])
        pack_sb = sb("pack_sb", [P, D + N_ROUTED])
        ctxT = sb("ctxT_sb", [P, B * KEYS])
        woT = pack_sb[:, 0:D]
        rwT = pack_sb[:, D:]
        bout_sb = sb("bout_sb", [KEYS, D])
        mean_mat = sb("mean_mat", [P, P])
        warm = sb("warm", [P, P], mybir.dt.bfloat16)
        ident = sb("ident", [P, P])
        sel_f = sb("sel_f", [2 * N_ROUTED, C - 1, P])
        sel = sb("sel", [2 * N_ROUTED, C - 1, P], f32r)
        up_f = sb("up_f", [P, C, P])
        up_hi = sb("up_hi", [P, C, P], f32r)
        up_lo = sb("up_lo", [P, C, P], f32r)
        down_f = sb("down_f", [P, C, D])
        down_hi = sb("down_hi", [P, C, D], f32r)
        down_lo = sb("down_lo", [P, C, D], f32r)
        kc = sb("kc", [P, B * KEYS])
        vproj = sb("vproj", [KEYS, B, D])
        mhalf = sb("mhalf", [P, J])
        bn1 = sb("bn1", [P, B, J, 6])
        mv1 = sb("mv1", [P, B, J, 2])
        var1 = sb("var1", [P, B, J])
        rs1 = sb("rs1", [P, B, J])
        nmax = sb("nmax", [P, B, J])
        nbias = sb("nbias", [P, B, J])
        prob = sb("prob", [P, B, J, KEYS])
        den = sb("den", [P, B, J])
        rden = sb("rden", [P, B, J])
        probT = sb("probT", [KEYS, B, S])
        x1 = sb("x1", [P, B, J, D])
        bn2 = sb("bn2", [P, B, J, 6])
        mv2 = sb("mv2", [P, B, J, 2])
        var2 = sb("var2", [P, B, J])
        rs2 = sb("rs2", [P, B, J])
        xn2 = sb("xn2", [P, B, J, D])
        xn_hi = sb("xn_hi", [P, B, S], f32r)
        xn_lo = sb("xn_lo", [P, B, S], f32r)
        xn_f = sb("xn_f", [P, 2, S])
        NSENT = 4
        lmax = sb("lmax", [P, B, J])
        dlog = sb("dlog", [P, B, J, N_ROUTED + NSENT])
        top = sb("top", [P, B, J, 12])
        left = sb("left", [P, B, J, N_ROUTED + NSENT])
        expl = sb("expl", [P, B, J, N_ROUTED])
        esum = sb("esum", [P, B, J])
        resum = sb("resum", [P, B, J])
        chosen = sb("chosen", [P, B, J, N_ROUTED])
        gnum = sb("gnum", [P, B, J, N_ROUTED])
        gate = sb("gate", [P, B, J, N_ROUTED])
        gate2 = sb("gate2", [P, B, J, 2, N_ROUTED], f32r)
        gateT = sb("gateT", [2 * N_ROUTED, B, S], f32r)
        act_r = sb("act_r", [P, N_ACT, S])
        gated_r = sb("gated_r", [P, N_GATED, S])
        hi_r = sb("hi_r", [P, N_PARTS, S], f32r)
        lo_r = sb("lo_r", [P, N_PARTS, S], f32r)
        ffnT = sb("ffnT", [P, 2, S])

        up_ps = [bank("up0"), bank("up1")]
        gb_ps = [bank("gb0"), bank("gb1")]
        down_ps, bank_a, bank_b, bank_c = bank("down"), bank("bank_a"), bank("bank_b"), bank("bank_c")
        score_ps = [bank_a, gb_ps[0], gb_ps[1], up_ps[0]]

        out_ps = [bank_c, bank_b]

        def parts(b):
            return [slice(0, J)] if b < B - 1 else [slice(0, J // 2), slice(J // 2, J)]

        kbar_ps = [up_ps[0], up_ps[1]]
        FIRST_KEYS, OTHER_KEYS = slice(0, KEYS), slice(KEYS, B * KEYS)

        def tiles(ps, w):
            return ps[:, 0:J * w].rearrange("p (j w) -> p j w", w=w)

        ld_ctx, ld_pack, ld_x0, ld_x1, ld_x, ld_xT0, ld_xT1, ld_xT = map(sem, (
            "ld_ctx", "ld_pack", "ld_x0", "ld_x1", "ld_x", "ld_xT0", "ld_xT1", "ld_xT"))
        ld_bout, ld_up, ld_down, ld_sel, ld_id = map(sem, ("ld_bout", "ld_up", "ld_down", "ld_sel", "ld_id"))
        mean_ready, warm_ready = sem("mean_ready"), sem("warm_ready")
        const_ready, kbar_done, kc_ready, vproj_done, vproj_ready = map(sem, (
            "const_ready", "kbar_done", "kc_ready", "vproj_done", "vproj_ready"))
        uphi_ready, uplo_ready, dnhi_ready, dnlo_ready, sel_ready = map(sem, (
            "uphi_ready", "uplo_ready", "dnhi_ready", "dnlo_ready", "sel_ready"))
        scores_done, bn1_tiles, mv1_tiles, var1_ready, rs1_ready = map(sem, (
            "scores_done", "bn1_tiles", "mv1_tiles", "var1_ready", "rs1_ready"))
        nmax_ready, nbias_ready, prob_tiles, probT_done, probT_ready = map(sem, (
            "nmax_ready", "nbias_ready", "prob_tiles", "probT_done", "probT_ready"))
        den_ready = sem("den_ready")
        attn_done, rden_ready, x1_tiles, bn2_tiles, mv2_tiles, var2_ready, rs2_ready, xn2_tiles = map(sem, (
            "attn_done", "rden_ready", "x1_tiles", "bn2_tiles", "mv2_tiles", "var2_ready", "rs2_ready", "xn2_tiles"))
        xnT_done, xnhi_ready, xnf_ready, xnlo_ready = map(sem, (
            "xnT_done", "xnhi_ready", "xnf_ready", "xnlo_ready"))
        logits_done, lmax_ready, dlog_ready, top_tiles, left_tiles, expl_ready = map(sem, (
            "logits_done", "lmax_ready", "dlog_ready", "top_tiles", "left_tiles", "expl_ready"))
        esum_ready, resum_ready, chosen_ready, gnum_ready, gate_ready, ghi_ready, glo_ready = map(sem, (
            "esum_ready", "resum_ready", "chosen_ready", "gnum_ready", "gate_ready", "ghi_ready", "glo_ready"))
        gateT_done, gateT_ready = map(sem, ("gateT_done", "gateT_ready"))
        up_chunks, act_chunks, gb_chunks, gated_chunks, hi_chunks, lo_chunks, down_chunks = map(sem, (
            "up_chunks", "act_chunks", "gb_chunks", "gated_chunks", "hi_chunks", "lo_chunks", "down_chunks"))
        ffnT_ready, outT_done, out_ready, stored = map(sem, ("ffnT_ready", "outT_done", "out_ready", "stored"))

        def source(g):
            if g % C == 0:
                return act_r[:, g % N_ACT, :]
            return gated_r[:, GATED.index(g) % N_GATED, :]

        def wait_source(eng, g):
            if g % C == 0:
                eng.wait_ge(act_chunks, g + 1)
            else:
                eng.wait_ge(gated_chunks, GATED.index(g) + 1)

        def wait_source_free(eng, g):
            eng.wait_ge(lo_chunks, g + 1)

        def high_part(eng, copy, g):
            if g >= N_PARTS:
                eng.wait_ge(down_chunks, g - N_PARTS + 1)
            if g and on_vector(g - 1) != on_vector(g):
                eng.wait_ge(hi_chunks, g)
            copy(hi_r[:, g % N_PARTS, :], source(g)).then_inc(hi_chunks, 1)

        def low_part(eng, subtract, g, done):
            eng.wait_ge(hi_chunks, g + 1)
            if g >= N_PARTS:
                eng.wait_ge(down_chunks, g - N_PARTS + 1)
            subtract(lo_r[:, g % N_PARTS, :], source(g), hi_r[:, g % N_PARTS, :].bitcast(f32),
                     ALU.subtract).then_inc(done, 1)

        block = ctx.enter_context(nc.Block())

        @block.sync
        def _(sp):
            sp.dma_start(ctxT[:, :], ctxT_in).then_inc(ld_ctx, 16)
            sp.dma_start(x_sb[:, 0, :, :], x[0]).then_inc(ld_x0, 16)
            sp.dma_start(xT_sb[:, 0, :], xT[:, 0, :]).then_inc(ld_xT0, 16)
            sp.dma_start(x_sb[:, 1, :, :], x[1]).then_inc(ld_x1, 16)
            sp.dma_start(pack_sb[:, :], attn_pack).then_inc(ld_pack, 16)
            sp.dma_start(ident[:, :], identity).then_inc(ld_id, 16)
            sp.dma_start(bout_sb[:, :], b_out.to_broadcast([KEYS, D])).then_inc(ld_bout, 16)
            sp.dma_start(xT_sb[:, 1, :], xT[:, 1, :]).then_inc(ld_xT1, 16)
            sp.dma_start(x_sb[:, 2:B, :, :], x[2:B].rearrange("b p j d -> p b j d")).then_inc(ld_x, 16)
            sp.dma_start(sel_f[:, :, :], selector).then_inc(ld_sel, 16)
            sp.dma_start(xT_sb[:, 2:B, :], xT[:, 2:B, :]).then_inc(ld_xT, 16)
            sp.dma_start(up_f[:, :, :], upT).then_inc(ld_up, 16)
            sp.dma_start(down_f[:, :, :], downT).then_inc(ld_down, 16)
            for b in range(B):
                for i, part in enumerate(parts(b)):
                    sp.wait_ge(out_ready, b + i + 1)
                    sp.dma_start(out[b, :, part, :], x1[:, b, part, :]).then_inc(stored, 16)
            sp.wait_ge(stored, 16 * (B + 1))

        @block.gpsimd
        def _(pool):
            pool.memset(mean_mat[:, :], 1.0 / D).then_inc(mean_ready, 1)
            pool.memset(warm[:, :], 0.0).then_inc(warm_ready, 1)
            pool.memset(mhalf[:, :], -0.5).then_inc(const_ready, 1)
            pool.memset(dlog[:, :, :, N_ROUTED:], -3.0e38).then_inc(const_ready, 1)
            pool.memset(top[:, :, :, 8:], -3.0e38).then_inc(const_ready, 1)
            pool.wait_ge(const_ready, 3)

            def rstd(b, mv, var, rs, mv_tiles, var_sem, rs_sem, factor):
                pool.wait_ge(mv_tiles, J * (b + 1))
                nc.gpsimd.tensor_scalar(var[:, b, :], mv[:, b, :, 1], EPS, factor,
                                        ALU.add, ALU.mult).then_inc(var_sem, 1)
                pool.wait_ge(var_sem, b + 1)
                nc.gpsimd.tensor_tensor(rs[:, b, :], var[:, b, :], mhalf[:, :], ALU.pow).then_inc(rs_sem, 1)

            def rstd1(b):
                rstd(b, mv1, var1, rs1, mv1_tiles, var1_ready, rs1_ready, float(D))

            def rstd2(b):
                rstd(b, mv2, var2, rs2, mv2_tiles, var2_ready, rs2_ready, 1.0)

            def up_low(c0, c1):
                nc.gpsimd.tensor_tensor(up_lo[:, c0:c1, :], up_f[:, c0:c1, :], up_hi[:, c0:c1, :].bitcast(f32),
                                        ALU.subtract).then_inc(uplo_ready, 1)

            rstd1(0)
            rstd1(1)
            rstd1(2)
            rstd2(0)
            rstd1(3)
            pool.wait_ge(uphi_ready, 1)
            up_low(0, UP_FIRST)
            pool.wait_ge(uphi_ready, 2)
            up_low(UP_FIRST, C)
            pool.wait_ge(dnhi_ready, 1)
            nc.gpsimd.tensor_tensor(down_lo[:, :, :], down_f[:, :, :], down_hi[:, :, :].bitcast(f32),
                                    ALU.subtract).then_inc(dnlo_ready, 1)
            for g in range(N_CHUNKS):
                if (b := stage_batch(g, RSTD)) is not None:
                    rstd2(b)
                if is_split(g):
                    low_part(pool, nc.gpsimd.tensor_tensor, g, lo_chunks)

        @block.scalar
        def _(act):
            nc.scalar.preload_act_table(ACT.Exp)

            def softmax_exp(b):
                act.wait_ge(scores_done, b + 1)
                act.wait_ge(nbias_ready, b + 1)
                for j in range(J):
                    nc.scalar.activation(prob[:, b, j, :], tiles(score_ps[b], KEYS)[:, j, :], ACT.Exp,
                                         bias=nbias[:, b, j:j + 1],
                                         scale=rs1[:, b, j:j + 1]).then_inc(prob_tiles, 1)

            def copy_probT(b):
                act.wait_ge(probT_done, b + 1)
                nc.scalar.copy(probT[:, b, :], bank_b[0:KEYS, :]).then_inc(probT_ready, 1)

            def copy_xnT(b):
                act.wait_ge(xnT_done, b + 1)
                if b >= 2:
                    act.wait_ge(logits_done, b - 1)
                    act.wait_ge(xnlo_ready, b - 1)
                nc.scalar.copy(xn_f[:, b % 2, :], bank_b[:, :]).then_inc(xnf_ready, 1)

            def router_exp(b):
                act.wait_ge(dlog_ready, b + 1)
                nc.scalar.activation(expl[:, b, :, :], dlog[:, b, :, 0:N_ROUTED], ACT.Exp).then_inc(expl_ready, 1)

            def copy_gateT(b):
                act.wait_ge(gateT_done, b + 1)
                nc.scalar.copy(gateT[:, b, :], bank_a[0:2 * N_ROUTED, :]).then_inc(gateT_ready, 1)

            def copy_ffnT(b):
                act.wait_ge(down_chunks, C * (b + 1))
                if b >= 2:
                    act.wait_ge(outT_done, b - 1)
                for part in parts(b):
                    tokens = slice(part.start * P, part.stop * P)
                    nc.scalar.copy(ffnT[:, b % 2, tokens], down_ps[:, tokens]).then_inc(ffnT_ready, 1)

            def up_high(c0, c1):
                nc.scalar.copy(up_hi[:, c0:c1, :], up_f[:, c0:c1, :]).then_inc(uphi_ready, 1)

            softmax_exp(0)
            copy_probT(0)
            act.wait_ge(ld_sel, 16)
            nc.scalar.copy(sel[:, :, :], sel_f[:, :, :]).then_inc(sel_ready, 1)
            softmax_exp(1)
            act.wait_ge(ld_up, 16)
            up_high(0, UP_FIRST)
            up_high(UP_FIRST, C)
            copy_probT(1)
            softmax_exp(2)
            act.wait_ge(ld_down, 16)
            nc.scalar.copy(down_hi[:, :, :], down_f[:, :, :]).then_inc(dnhi_ready, 1)
            copy_xnT(0)
            softmax_exp(3)
            router_exp(0)
            for g in range(N_CHUNKS + LAG + 2):
                if g < N_CHUNKS:
                    if (b := stage_batch(g, PROBT)) is not None:
                        copy_probT(b)
                    if (b := stage_batch(g, XNT)) is not None:
                        copy_xnT(b)
                    if (b := stage_batch(g, EXPL)) is not None:
                        router_exp(b)
                    if (b := stage_batch(g, GATET)) is not None:
                        copy_gateT(b)
                    act.wait_ge(up_chunks, g + 1)
                    if g >= N_ACT:
                        if (g - N_ACT) % C:
                            act.wait_ge(gated_chunks, GATED.index(g - N_ACT) + 1)
                        else:
                            wait_source_free(act, g - N_ACT)
                    nc.scalar.activation(act_r[:, g % N_ACT, :], up_ps[g % 2][:, :], ACT.Gelu).then_inc(act_chunks, 1)
                    if g == GATE0_COPY:
                        copy_gateT(0)
                if g >= 1 and is_split(g - 1) and not on_vector(g - 1):
                    wait_source(act, g - 1)
                    high_part(act, nc.scalar.copy, g - 1)
                if (b := finished_batch(g, 0)) is not None:
                    copy_ffnT(b)

        @block.vector
        def _(dve):
            def stats(b, src, bn, mv, bn_sem, mv_sem):
                for j in range(J):
                    if src is x1:
                        dve.wait_ge(x1_tiles, J * b + j + 1)
                    nc.vector.bn_stats(bn[:, b, j, :], src[:, b, j, :]).then_inc(bn_sem, 1)
                for j in range(J):
                    dve.wait_ge(bn_sem, J * b + j + 1)
                    nc.vector.bn_aggr(mv[:, b, j, :], bn[:, b, j, :]).then_inc(mv_sem, 1)

            def attention_head(b):
                dve.wait_ge(scores_done, b + 1)
                nc.vector.tensor_reduce(nmax[:, b, :], tiles(score_ps[b], KEYS), AX.X, ALU.max,
                                        negate=True).then_inc(nmax_ready, 1)
                dve.wait_ge(nmax_ready, b + 1)
                dve.wait_ge(rs1_ready, b + 1)
                nc.vector.tensor_tensor(nbias[:, b, :], nmax[:, b, :], rs1[:, b, :],
                                        ALU.mult).then_inc(nbias_ready, 1)

            def denominator(b):
                dve.wait_ge(prob_tiles, J * (b + 1))
                nc.vector.tensor_reduce(den[:, b, :], prob[:, b, :, :], AX.X, ALU.add).then_inc(den_ready, 1)
                dve.wait_ge(den_ready, b + 1)
                nc.vector.reciprocal(rden[:, b, :], den[:, b, :]).then_inc(rden_ready, 1)

            def attention_out(b):
                dve.wait_ge(attn_done, b + 1)
                dve.wait_ge(rden_ready, b + 1)
                for j in range(J):
                    nc.vector.scalar_tensor_tensor(x1[:, b, j, :], tiles(bank_c, D)[:, j, :], rden[:, b, j:j + 1],
                                                   x_sb[:, b, j, :], ALU.mult, ALU.add).then_inc(x1_tiles, 1)

            def stats1(b):
                dve.wait_ge((ld_x0, ld_x1, ld_x)[min(b, 2)], 16)
                stats(b, x_sb, bn1, mv1, bn1_tiles, mv1_tiles)

            def stats2(b):
                stats(b, x1, bn2, mv2, bn2_tiles, mv2_tiles)

            def normalize(b):
                dve.wait_ge(mv2_tiles, J * (b + 1))
                dve.wait_ge(rs2_ready, b + 1)
                for j in range(J):
                    nc.vector.tensor_scalar(xn2[:, b, j, :], x1[:, b, j, :], mv2[:, b, j, 0:1], rs2[:, b, j:j + 1],
                                            ALU.subtract, ALU.mult).then_inc(xn2_tiles, 1)

            def split_xnT(b):
                dve.wait_ge(xnf_ready, b + 1)
                nc.vector.tensor_copy(xn_hi[:, b, :], xn_f[:, b % 2, :]).then_inc(xnhi_ready, 1)
                dve.wait_ge(xnhi_ready, b + 1)
                nc.vector.tensor_tensor(xn_lo[:, b, :], xn_f[:, b % 2, :], xn_hi[:, b, :].bitcast(f32),
                                        ALU.subtract).then_inc(xnlo_ready, 1)

            def spread(v):
                return v.unsqueeze(2).to_broadcast([P, J, N_ROUTED])

            def router_choose(b):
                dve.wait_ge(logits_done, b + 1)
                logits = tiles(bank_a, N_ROUTED)
                nc.vector.tensor_reduce(lmax[:, b, :], logits, AX.X, ALU.max).then_inc(lmax_ready, 1)
                dve.wait_ge(lmax_ready, b + 1)
                if b == 0:
                    dve.wait_ge(const_ready, 3)
                nc.vector.tensor_tensor(dlog[:, b, :, 0:N_ROUTED], logits, spread(lmax[:, b, :]),
                                        ALU.subtract).then_inc(dlog_ready, 1)
                dve.wait_ge(dlog_ready, b + 1)
                for j in range(J):
                    nc.vector.max(top[:, b, j, 0:8], dlog[:, b, j, 0:N_ROUTED]).then_inc(top_tiles, 1)
                for j in range(J):
                    dve.wait_ge(top_tiles, J * b + j + 1)
                    four = top[:, b, j, :].rearrange("p (a k) -> p a k", k=TOP_K)[:, 0:3:2, :]
                    nc.vector.match_replace(left[:, b, j, :], four, dlog[:, b, j, :], 1.0).then_inc(left_tiles, 1)

            def router_gate(b):
                dve.wait_ge(left_tiles, J * (b + 1))
                nc.vector.tensor_tensor(chosen[:, b, :, :], left[:, b, :, 0:N_ROUTED], dlog[:, b, :, 0:N_ROUTED],
                                        ALU.not_equal).then_inc(chosen_ready, 1)
                dve.wait_ge(expl_ready, b + 1)
                nc.vector.tensor_reduce(esum[:, b, :], expl[:, b, :, :], AX.X, ALU.add).then_inc(esum_ready, 1)
                dve.wait_ge(chosen_ready, b + 1)
                nc.vector.tensor_tensor(gnum[:, b, :, :], chosen[:, b, :, :], expl[:, b, :, :],
                                        ALU.mult).then_inc(gnum_ready, 1)
                dve.wait_ge(esum_ready, b + 1)
                nc.vector.reciprocal(resum[:, b, :], esum[:, b, :]).then_inc(resum_ready, 1)
                dve.wait_ge(gnum_ready, b + 1)
                dve.wait_ge(resum_ready, b + 1)
                nc.vector.tensor_tensor(gate[:, b, :, :], gnum[:, b, :, :], spread(resum[:, b, :]),
                                        ALU.mult).then_inc(gate_ready, 1)
                dve.wait_ge(gate_ready, b + 1)
                nc.vector.tensor_copy(gate2[:, b, :, 0, :], gate[:, b, :, :]).then_inc(ghi_ready, 1)
                dve.wait_ge(ghi_ready, b + 1)
                nc.vector.tensor_tensor(gate2[:, b, :, 1, :], gate[:, b, :, :], gate2[:, b, :, 0, :].bitcast(f32),
                                        ALU.subtract).then_inc(glo_ready, 1)

            def finish(b):
                for i, part in enumerate(parts(b)):
                    dve.wait_ge(outT_done, b + i + 1)
                    nc.vector.tensor_tensor(x1[:, b, part, :], tiles(out_ps[i], D)[:, part, :],
                                            x1[:, b, part, :], ALU.add).then_inc(out_ready, 1)

            def center_context(keys, done):
                dve.wait_ge(kbar_done, done)
                nc.vector.tensor_tensor(kc[:, keys], ctxT[:, keys], kbar_ps[done - 1][:, keys],
                                        ALU.subtract).then_inc(kc_ready, 1)

            dve.wait_ge(ld_ctx, 16)
            center_context(FIRST_KEYS, 1)
            stats1(0)
            center_context(OTHER_KEYS, 2)
            attention_head(0)
            stats1(1)
            dve.wait_ge(vproj_done, 1)
            dve.wait_ge(ld_bout, 16)
            nc.vector.tensor_tensor(vproj[:, :, :], tiles(up_ps[1], D)[0:KEYS, :, :],
                                    bout_sb[:, :].unsqueeze(1).to_broadcast([KEYS, B, D]),
                                    ALU.add).then_inc(vproj_ready, 1)
            denominator(0)
            stats1(2)
            attention_head(1)
            attention_out(0)
            stats2(0)
            attention_head(2)
            stats1(3)
            normalize(0)
            attention_head(3)
            split_xnT(0)
            router_choose(0)
            router_gate(0)
            denominator(1)
            attention_out(1)
            if STATS[0] < 0:
                stats2(1)
            for g in range(N_CHUNKS + LAG + 3):
                if (b := stage_batch(g, SPLIT)) is not None:
                    split_xnT(b)
                if (b := stage_batch(g, CHOOSE)) is not None:
                    router_choose(b)
                if (b := stage_batch(g, GATE)) is not None:
                    router_gate(b)
                if g < N_CHUNKS and g % C:
                    r = GATED.index(g)
                    dve.wait_ge(act_chunks, g + 1)
                    dve.wait_ge(gb_chunks, r + 1)
                    if r >= N_GATED:
                        wait_source_free(dve, GATED[r - N_GATED])
                    nc.vector.tensor_tensor(gated_r[:, r % N_GATED, :], act_r[:, g % N_ACT, :],
                                            gb_ps[r % 2][:, :], ALU.mult).then_inc(gated_chunks, 1)
                    if is_split(g) and on_vector(g):
                        dve.wait_ge(gated_chunks, r + 1)
                        high_part(dve, nc.vector.tensor_copy, g)
                if (b := stage_batch(g, X1)) is not None:
                    denominator(b)
                    attention_out(b)
                if (b := stage_batch(g, STATS)) is not None:
                    stats2(b)
                if (b := stage_batch(g, NORM)) is not None:
                    normalize(b)
                if (b := finished_batch(g, OUT_AFTER)) is not None:
                    finish(b)

        @block.tensor
        def _(pe):
            def scores(b):
                pe.wait_ge((ld_xT0, ld_xT1, ld_xT)[min(b, 2)], 16)
                for j in range(J):
                    last = nc.tensor.matmul(tiles(score_ps[b], KEYS)[:, j, :], xT_sb[:, b, j * P:(j + 1) * P],
                                            kc[:, b * KEYS:(b + 1) * KEYS], start=True, stop=True)
                last.then_inc(scores_done, 1)

            def pe_out_left(g):
                n = sum(C * (b + 1) - 1 + LAG + OUT_AFTER < g for b in range(B))
                if n:
                    pe.wait_ge(out_ready, n)

            def transpose_prob(b):
                if b == 0:
                    pe.wait_ge(ld_id, 16)
                elif b == 1:
                    pe.wait_ge(probT_ready, 1)
                else:
                    pe.wait_ge(xnf_ready, b)
                for j in range(J):
                    pe.wait_ge(prob_tiles, J * b + j + 1)
                    last = nc.tensor.transpose(bank_b[0:KEYS, j * P:(j + 1) * P], prob[:, b, j, :], ident[:, :])
                last.then_inc(probT_done, 1)

            def attend(b):
                pe.wait_ge(probT_ready, b + 1)
                if b == 0:
                    pe.wait_ge(vproj_ready, 1)
                if b:
                    pe.wait_ge(x1_tiles, J * b)
                pe_out_left(ATTN[b - 1] if b else -1)
                for j in range(J):
                    last = nc.tensor.matmul(tiles(bank_c, D)[:, j, :], probT[:, b, j * P:(j + 1) * P],
                                            vproj[:, b, :], start=True, stop=True)
                last.then_inc(attn_done, 1)

            def transpose_xn(b):
                pe.wait_ge(probT_ready, max(b + 1, 2))
                for j in range(J):
                    pe.wait_ge(xn2_tiles, J * b + j + 1)
                    last = nc.tensor.transpose(bank_b[:, j * P:(j + 1) * P], xn2[:, b, j, :], ident[:, :])
                last.then_inc(xnT_done, 1)

            def logits(b):
                pe.wait_ge(xnf_ready, b + 1)
                if b >= 1:
                    pe.wait_ge(gateT_ready, b)
                for j in range(J):
                    last = nc.tensor.matmul(tiles(bank_a, N_ROUTED)[:, j, :], xn_f[:, b % 2, j * P:(j + 1) * P],
                                            rwT, start=True, stop=True)
                last.then_inc(logits_done, 1)

            def transpose_gate(b):
                pe.wait_ge(glo_ready, b + 1)
                for j in range(J):
                    last = nc.tensor.transpose(
                        bank_a[0:2 * N_ROUTED, j * P:(j + 1) * P],
                        gate2[:, b, j, :, :].bitcast(f32).rearrange("p a e -> p (a e)"), ident[:, :])
                last.then_inc(gateT_done, 1)

            def up(g):
                b, c = g // C, g % C
                if g < C:
                    pe.wait_ge(uplo_ready, 1 if c < UP_FIRST else 2)
                if c == 0:
                    pe.wait_ge(xnlo_ready, b + 1)
                if g >= 2:
                    pe.wait_ge(act_chunks, g - 1)
                nc.tensor.matmul(up_ps[g % 2][:, :], up_hi[:, c, :], xn_hi[:, b, :], start=True, stop=False)
                nc.tensor.matmul(up_ps[g % 2][:, :], up_hi[:, c, :], xn_lo[:, b, :], start=False, stop=False)
                nc.tensor.matmul(up_ps[g % 2][:, :], up_lo[:, c, :], xn_hi[:, b, :], start=False,
                                 stop=True).then_inc(up_chunks, 1)

            def spread_gate(g):
                b, c = g // C, g % C
                if c == 0:
                    return
                r = GATED.index(g)
                if c == 1:
                    pe.wait_ge(gateT_ready, b + 1)
                if g == 1:
                    pe.wait_ge(sel_ready, 1)
                if r >= 2:
                    pe.wait_ge(gated_chunks, r - 1)
                nc.tensor.matmul(gb_ps[r % 2][:, :], sel[:, c - 1, :], gateT[:, b, :], start=True,
                                 stop=True).then_inc(gb_chunks, 1)

            def down(g):
                b, c = g // C, g % C
                if c == 0 and b:
                    pe.wait_ge(ffnT_ready, b)
                first, last = c == 0, c == C - 1
                if is_split(g):
                    pe.wait_ge(lo_chunks, g + 1)
                    hi, lo = hi_r[:, g % N_PARTS, :], lo_r[:, g % N_PARTS, :]
                    nc.tensor.matmul(down_ps[:, :], down_hi[:, c, :], hi, start=first, stop=False)
                    nc.tensor.matmul(down_ps[:, :], down_lo[:, c, :], hi, start=False, stop=False)
                    mm = nc.tensor.matmul(down_ps[:, :], down_hi[:, c, :], lo, start=False, stop=last)
                else:
                    wait_source(pe, g)
                    mm = nc.tensor.matmul(down_ps[:, :], down_f[:, c, :], source(g), start=first, stop=last)
                mm.then_inc(down_chunks, 1)

            def transpose_out(b):
                slot = C * (b + 1) - 1 + LAG + OUT_AFTER
                pe.wait_ge(x1_tiles, J * (1 + sum(at <= slot for at in ATTN)))
                pe_out_left(slot)
                for i, part in enumerate(parts(b)):
                    pe.wait_ge(ffnT_ready, b + i + 1)
                    for j in range(part.start, part.stop):
                        last = nc.tensor.transpose(tiles(out_ps[i], D)[:, j, :], ffnT[:, b % 2, j * P:(j + 1) * P],
                                                   ident[:, :])
                    last.then_inc(outT_done, 1)

            def keep_warm(n):
                for _ in range(n):
                    nc.tensor.matmul(down_ps[:, 0:P], warm[:, :], warm[:, :], start=True, stop=True)

            pe.wait_ge(warm_ready, 1)
            keep_warm(20)
            pe.wait_ge(mean_ready, 1)
            pe.wait_ge(ld_ctx, 16)
            for keys, ps in zip((FIRST_KEYS, OTHER_KEYS), kbar_ps):
                nc.tensor.matmul(ps[:, keys], mean_mat[:, :], ctxT[:, keys], start=True,
                                 stop=True).then_inc(kbar_done, 1)
            keep_warm(2)
            pe.wait_ge(kc_ready, 1)
            scores(0)
            pe.wait_ge(kc_ready, 2)
            pe.wait_ge(ld_pack, 16)
            for b in range(B):
                last = nc.tensor.matmul(tiles(up_ps[1], D)[0:KEYS, b, :], ctxT[:, b * KEYS:(b + 1) * KEYS], woT,
                                        start=True, stop=True)
            last.then_inc(vproj_done, 1)
            transpose_prob(0)
            scores(1)
            keep_warm(2)
            attend(0)
            scores(2)
            scores(3)
            transpose_prob(1)
            keep_warm(4)
            attend(1)
            keep_warm(5)
            transpose_xn(0)
            keep_warm(1)
            logits(0)
            pe.wait_ge(prob_tiles, J * B)
            for g in range(N_CHUNKS + LAG + 3):
                if (b := stage_batch(g, PROBT)) is not None:
                    transpose_prob(b)
                if (b := stage_batch(g, ATTN)) is not None:
                    attend(b)
                if (b := stage_batch(g, XNT)) is not None:
                    transpose_xn(b)
                if (b := stage_batch(g, LOGITS)) is not None:
                    logits(b)
                if (b := stage_batch(g, GATET)) is not None:
                    transpose_gate(b)
                if (b := finished_batch(g, OUT_AFTER)) is not None:
                    transpose_out(b)
                if g < N_CHUNKS:
                    up(g)
                if g == GATE0:
                    transpose_gate(0)
                if 0 <= g - SPREAD_LAG < N_CHUNKS:
                    spread_gate(g - SPREAD_LAG)
                if 0 <= g - LAG < N_CHUNKS:
                    if g == LAG:
                        pe.wait_ge(dnlo_ready, 1)
                    down(g - LAG)


def kernel(x, ctx_1024, L0_xattn_W_out, L0_xattn_b_out, L0_ffn_shared_up, L0_ffn_shared_down,
           L0_ffn_routed_up, L0_ffn_routed_down, L0_ffn_router_w):
    import numpy as np
    import concourse.bacc as bacc
    from concourse.bass_utils import run_bass_kernel_spmd

    x = np.asarray(x)
    tiles = x.reshape(B, P, J, D)
    up = np.concatenate([np.asarray(L0_ffn_shared_up), np.asarray(L0_ffn_routed_up)])
    down = np.concatenate([np.asarray(L0_ffn_shared_down), np.asarray(L0_ffn_routed_down)])
    selector = np.zeros((2, N_ROUTED, C - 1, P), np.float32)
    for c in range(C - 1):
        for m in range(P):
            selector[:, (c * P + m) // E_DIM, c, m] = 1.0
    arrays = {
        "xT": tiles.transpose(3, 0, 2, 1).reshape(D, B, S),
        "x": tiles,
        "ctxT": np.asarray(ctx_1024).transpose(2, 0, 1).reshape(D, B * KEYS),
        "attn_pack": np.concatenate([np.asarray(L0_xattn_W_out).T, np.asarray(L0_ffn_router_w).T], axis=1),
        "b_out": np.asarray(L0_xattn_b_out).reshape(1, D),
        "upT": up.reshape(C, P, D).transpose(2, 0, 1),
        "downT": down.transpose(0, 2, 1).reshape(C, P, D).transpose(1, 0, 2),
        "selector": selector.reshape(2 * N_ROUTED, C - 1, P),
        "identity": np.eye(P, dtype=np.float32),
    }
    arrays = {k + "_dram": np.ascontiguousarray(v) for k, v in arrays.items()}
    nc = bacc.Bacc("TRN2", target_bir_lowering=False, num_devices=1)
    args = [nc.dram_tensor(k, v.shape, mybir.dt.float32, kind="ExternalInput").ap() for k, v in arrays.items()]
    out = nc.dram_tensor("out_dram", (B, P, J, D), mybir.dt.float32, kind="ExternalOutput").ap()
    xattn_moe_kernel(nc, *args, out)
    r = run_bass_kernel_spmd(nc, [arrays], core_ids=[0])
    return r.results[0]["out_dram"].reshape(B, S, D)
```
